# Optimizing a Trainium2 kernel written in Bass

```python
import numpy as np
import jax
import jax.numpy as jnp

def _softmax(x, axis=-1):
    return jax.nn.softmax(x, axis=axis)
def _gelu(x):
    return jax.nn.gelu(x, approximate=True)
def _silu(x):
    return jax.nn.silu(x)
def _sigmoid(x):
    return jax.nn.sigmoid(x)
def _layernorm(x, axis=-1, eps=1e-5):
    m = jnp.mean(x, axis=axis, keepdims=True)
    v = jnp.var(x, axis=axis, keepdims=True)
    return (x - m) / jnp.sqrt(v + eps)
def _scatter_add(tgt, idx, src, axis=0):
    return tgt.at[idx].add(src)
def _segment_sum(src, seg, n):
    return jax.ops.segment_sum(src, seg, n)

kernel_name = 'mk_conv_attn_hybrid_d2_conv_nchw128_de4b7c'

def setup_inputs(seed: int = 0):
    np.random.seed(seed)
    _w = jnp.asarray
    def _rec_inputs():
        import jax
        import jax.numpy as jnp
        _gk = jax.random.key(seed)
        x = -3.205e-05 + 1 * jax.random.normal(jax.random.fold_in(_gk, 1), (32, 128, 64, 22), jnp.float32)
        return x
    x = _rec_inputs()
    def _L0_conv_setup():
        import jax, jax.numpy as jnp
        import numpy as np
        C = 128
        D_STATE = 16
        D_CONV = 4
        EXPAND = 2
        DI = EXPAND * C
        DT_RANK = (C + 15) // 16
        NM, T, V = (32, 64, 22)

        def _mamba(x, in_w, conv_w, conv_b, xproj_w, dt_w, dt_b, Alog, Dp, out_w):
            B_, L, _ = x.shape
            xz = x @ in_w.T
            xi, z = jnp.split(xz, 2, axis=-1)
            K = conv_w.shape[-1]
            xp = jnp.pad(xi, ((0, 0), (K - 1, 0), (0, 0)))
            xc = conv_b + sum((xp[:, k:k + L, :] * conv_w[:, k] for k in range(K)))
            xc = jax.nn.silu(xc)
            dbl = xc @ xproj_w.T
            dt, Bm, Cm = jnp.split(dbl, [DT_RANK, DT_RANK + D_STATE], axis=-1)
            dt = jax.nn.softplus(dt @ dt_w.T + dt_b)
            A = -jnp.exp(Alog)

            def step(h, inp):
                dt_l, B_l, C_l, u_l = inp
                dA = jnp.exp(dt_l[:, :, None] * A)
                h = dA * h + (dt_l * u_l)[:, :, None] * B_l[:, None, :]
                y = jnp.einsum('bds,bs->bd', h, C_l)
                return (h, y)
            h0 = jnp.zeros((B_, DI, D_STATE), x.dtype)
            xs = (jnp.moveaxis(dt, 1, 0), jnp.moveaxis(Bm, 1, 0), jnp.moveaxis(Cm, 1, 0), jnp.moveaxis(xc, 1, 0))
            _, ys = jax.lax.scan(step, h0, xs)
            y = jnp.moveaxis(ys, 0, 1) + xc * Dp
            y = y * jax.nn.silu(z)
            return y @ out_w.T
        key = jax.random.key(seed)
        ks = jax.random.split(key, 40)
        i = [0]

        def nrm(shape, s=0.05):
            i[0] += 1
            return jax.random.normal(ks[i[0]], shape, jnp.float32) * s
        inp = {'x': jax.random.normal(ks[0], (NM, C, T, V), jnp.float32)}
        for p in ('f', 'b'):
            inp[p + '_in_w'] = nrm((2 * DI, C))
            inp[p + '_conv_w'] = nrm((DI, D_CONV), 0.2)
            inp[p + '_conv_b'] = nrm((DI,))
            inp[p + '_xproj_w'] = nrm((DT_RANK + 2 * D_STATE, DI))
            inp[p + '_dt_w'] = nrm((DI, DT_RANK), 0.1)
            inp[p + '_dt_b'] = nrm((DI,), 0.1)
            i[0] += 1
            inp[p + '_Alog'] = jax.random.uniform(ks[i[0]], (DI, D_STATE), jnp.float32)
            inp[p + '_D'] = nrm((DI,), 1.0)
            inp[p + '_out_w'] = nrm((C, DI))
        inp['fuse_w'] = nrm((C, 2 * C))
        inp['ln_w'] = jnp.ones((C,), jnp.float32)
        inp['ln_b'] = jnp.zeros((C,), jnp.float32)
        return inp
    _L0_conv_all = _L0_conv_setup()
    _L0_conv_in = {k: v for k, v in _L0_conv_all.items() if k in ('f_in_w', 'f_conv_w', 'f_conv_b', 'f_xproj_w', 'f_dt_w', 'f_dt_b', 'f_Alog', 'f_D', 'f_out_w', 'b_in_w', 'b_conv_w', 'b_conv_b', 'b_xproj_w', 'b_dt_w', 'b_dt_b', 'b_Alog', 'b_D', 'b_out_w', 'fuse_w', 'ln_w', 'ln_b', )}
    del _L0_conv_all

    def _L1_attn_setup():
        import jax, jax.numpy as jnp
        import numpy as np
        B, S, H, A = (8, 1024, 128, 16)
        key = jax.random.key(seed)
        ks = jax.random.split(key, 5)
        scale = 1.0 / np.sqrt(2 * H)
        return {'x': jax.random.normal(ks[0], (B, S, H), dtype=jnp.float32), 'W1': jax.random.normal(ks[1], (2 * H, A), dtype=jnp.float32) * scale, 'b1': jax.random.normal(ks[2], (A,), dtype=jnp.float32) * scale, 'w2': jax.random.normal(ks[3], (A, 1), dtype=jnp.float32) * (1.0 / np.sqrt(A)), 'b2': jax.random.normal(ks[4], (1,), dtype=jnp.float32) * (1.0 / np.sqrt(A))}
    _L1_attn_all = _L1_attn_setup()
    _L1_attn_in = {k: v for k, v in _L1_attn_all.items() if k in ('W1', 'b1', 'w2', 'b2', )}
    del _L1_attn_all

    def _L1_ffn_setup():
        import jax, jax.numpy as jnp
        import numpy as np
        B, N, D, C, E, K = (8, 8192, 128, 128, 8, 2)
        key = jax.random.key(seed)
        k0, k1, k2 = jax.random.split(key, 3)
        x = jax.random.normal(k0, (B, N, D), dtype=jnp.float32)
        router_w = jax.random.normal(k1, (D, E), dtype=jnp.float32) * 0.05
        router_b = jnp.zeros((E,), dtype=jnp.float32)
        expert_w = jax.random.normal(k2, (E, D, C), dtype=jnp.float32) * (1.0 / np.sqrt(D))
        expert_b = jnp.zeros((E, C), dtype=jnp.float32)
        return {'x': x, 'router_w': router_w, 'router_b': router_b, 'expert_w': expert_w, 'expert_b': expert_b}
    _L1_ffn_all = _L1_ffn_setup()
    _L1_ffn_in = {k: v for k, v in _L1_ffn_all.items() if k in ('router_w', 'router_b', 'expert_w', 'expert_b', )}
    del _L1_ffn_all

    return {
        "x": x,
        "L0_conv_f_in_w": _L0_conv_in["f_in_w"],
        "L0_conv_f_conv_w": _L0_conv_in["f_conv_w"],
        "L0_conv_f_conv_b": _L0_conv_in["f_conv_b"],
        "L0_conv_f_xproj_w": _L0_conv_in["f_xproj_w"],
        "L0_conv_f_dt_w": _L0_conv_in["f_dt_w"],
        "L0_conv_f_dt_b": _L0_conv_in["f_dt_b"],
        "L0_conv_f_Alog": _L0_conv_in["f_Alog"],
        "L0_conv_f_D": _L0_conv_in["f_D"],
        "L0_conv_f_out_w": _L0_conv_in["f_out_w"],
        "L0_conv_b_in_w": _L0_conv_in["b_in_w"],
        "L0_conv_b_conv_w": _L0_conv_in["b_conv_w"],
        "L0_conv_b_conv_b": _L0_conv_in["b_conv_b"],
        "L0_conv_b_xproj_w": _L0_conv_in["b_xproj_w"],
        "L0_conv_b_dt_w": _L0_conv_in["b_dt_w"],
        "L0_conv_b_dt_b": _L0_conv_in["b_dt_b"],
        "L0_conv_b_Alog": _L0_conv_in["b_Alog"],
        "L0_conv_b_D": _L0_conv_in["b_D"],
        "L0_conv_b_out_w": _L0_conv_in["b_out_w"],
        "L0_conv_fuse_w": _L0_conv_in["fuse_w"],
        "L0_conv_ln_w": _L0_conv_in["ln_w"],
        "L0_conv_ln_b": _L0_conv_in["ln_b"],
        "L1_attn_W1": _L1_attn_in["W1"],
        "L1_attn_b1": _L1_attn_in["b1"],
        "L1_attn_w2": _L1_attn_in["w2"],
        "L1_attn_b2": _L1_attn_in["b2"],
        "L1_ffn_router_w": _L1_ffn_in["router_w"],
        "L1_ffn_router_b": _L1_ffn_in["router_b"],
        "L1_ffn_expert_w": _L1_ffn_in["expert_w"],
        "L1_ffn_expert_b": _L1_ffn_in["expert_b"],
    }

def reference(x, L0_conv_f_in_w, L0_conv_f_conv_w, L0_conv_f_conv_b, L0_conv_f_xproj_w, L0_conv_f_dt_w, L0_conv_f_dt_b, L0_conv_f_Alog, L0_conv_f_D, L0_conv_f_out_w, L0_conv_b_in_w, L0_conv_b_conv_w, L0_conv_b_conv_b, L0_conv_b_xproj_w, L0_conv_b_dt_w, L0_conv_b_dt_b, L0_conv_b_Alog, L0_conv_b_D, L0_conv_b_out_w, L0_conv_fuse_w, L0_conv_ln_w, L0_conv_ln_b, L1_attn_W1, L1_attn_b1, L1_attn_w2, L1_attn_b2, L1_ffn_router_w, L1_ffn_router_b, L1_ffn_expert_w, L1_ffn_expert_b):
    import jax
    import jax.numpy as jnp
    def _L0_conv_ref(x, f_in_w, f_conv_w, f_conv_b, f_xproj_w, f_dt_w, f_dt_b, f_Alog, f_D, f_out_w, b_in_w, b_conv_w, b_conv_b, b_xproj_w, b_dt_w, b_dt_b, b_Alog, b_D, b_out_w, fuse_w, ln_w, ln_b):
        import jax, jax.numpy as jnp
        import numpy as np
        C = 128
        D_STATE = 16
        D_CONV = 4
        EXPAND = 2
        DI = EXPAND * C
        DT_RANK = (C + 15) // 16
        NM, T, V = (32, 64, 22)

        def _mamba(x, in_w, conv_w, conv_b, xproj_w, dt_w, dt_b, Alog, Dp, out_w):
            B_, L, _ = x.shape
            xz = x @ in_w.T
            xi, z = jnp.split(xz, 2, axis=-1)
            K = conv_w.shape[-1]
            xp = jnp.pad(xi, ((0, 0), (K - 1, 0), (0, 0)))
            xc = conv_b + sum((xp[:, k:k + L, :] * conv_w[:, k] for k in range(K)))
            xc = jax.nn.silu(xc)
            dbl = xc @ xproj_w.T
            dt, Bm, Cm = jnp.split(dbl, [DT_RANK, DT_RANK + D_STATE], axis=-1)
            dt = jax.nn.softplus(dt @ dt_w.T + dt_b)
            A = -jnp.exp(Alog)

            def step(h, inp):
                dt_l, B_l, C_l, u_l = inp
                dA = jnp.exp(dt_l[:, :, None] * A)
                h = dA * h + (dt_l * u_l)[:, :, None] * B_l[:, None, :]
                y = jnp.einsum('bds,bs->bd', h, C_l)
                return (h, y)
            h0 = jnp.zeros((B_, DI, D_STATE), x.dtype)
            xs = (jnp.moveaxis(dt, 1, 0), jnp.moveaxis(Bm, 1, 0), jnp.moveaxis(Cm, 1, 0), jnp.moveaxis(xc, 1, 0))
            _, ys = jax.lax.scan(step, h0, xs)
            y = jnp.moveaxis(ys, 0, 1) + xc * Dp
            y = y * jax.nn.silu(z)
            return y @ out_w.T
        nm, c, t, v = x.shape
        xs = jnp.transpose(x, (0, 2, 3, 1)).reshape(nm * t, v, c)
        fwd = _mamba(xs, f_in_w, f_conv_w, f_conv_b, f_xproj_w, f_dt_w, f_dt_b, f_Alog, f_D, f_out_w)
        bwd = _mamba(xs[:, ::-1, :], b_in_w, b_conv_w, b_conv_b, b_xproj_w, b_dt_w, b_dt_b, b_Alog, b_D, b_out_w)[:, ::-1, :]
        y = jnp.concatenate([fwd, bwd], axis=-1) @ fuse_w.T
        mu = y.mean(-1, keepdims=True)
        var = y.var(-1, keepdims=True)
        y = (y - mu) / jnp.sqrt(var + 1e-05) * ln_w + ln_b
        return jnp.transpose(y.reshape(nm, t, v, c), (0, 3, 1, 2))

    def _L1_attn_ref(x, W1, b1, w2, b2):
        import jax, jax.numpy as jnp
        import numpy as np
        B, S, H, A = (8, 1024, 128, 16)
        h = x.shape[-1]
        f = jnp.einsum('bih,ha->bia', x, W1[:h])
        g = jnp.einsum('bjh,ha->bja', x, W1[h:])
        t = jnp.tanh(f[:, :, None, :] + g[:, None, :, :] + b1)
        scores = jnp.einsum('bija,a->bij', t, w2[:, 0]) + b2[0]
        n_seq = x.shape[1]
        flag = jnp.tril(jnp.ones((n_seq, n_seq), dtype=x.dtype), -1)[None, :, :]
        e = jnp.exp(scores) * flag
        denom = jnp.sum(e, axis=-1, keepdims=True) + 1e-10
        w = e / denom
        return jnp.einsum('bij,bjh->bih', w, x)

    def _L1_ffn_ref(x, router_w, router_b, expert_w, expert_b):
        import jax, jax.numpy as jnp
        import numpy as np
        B, N, D, C, E, K = (8, 8192, 128, 128, 8, 2)
        router_probs = jax.nn.softmax(x @ router_w + router_b, axis=-1)
        top_p, top_i = jax.lax.top_k(router_probs, K)
        top_p = top_p / jnp.sum(top_p, axis=-1, keepdims=True)
        expert_out = jnp.einsum('bnd,edc->bnec', x, expert_w) + expert_b
        gathered = jnp.take_along_axis(expert_out, top_i[..., None], axis=2)
        return jnp.einsum('bnk,bnkc->bnc', top_p, gathered)

    def _gn(v, G=32, eps=1e-5):
        B_, C_, H_, W_ = v.shape
        g = v.reshape(B_, G, C_ // G, H_, W_)
        m = jnp.mean(g, axis=(2, 3, 4), keepdims=True)
        s = jnp.var(g, axis=(2, 3, 4), keepdims=True)
        return ((g - m) / jnp.sqrt(s + eps)).reshape(v.shape)

    def _ln_c(v, eps=1e-6):
        m = jnp.mean(v, axis=1, keepdims=True)
        s = jnp.var(v, axis=1, keepdims=True)
        return (v - m) / jnp.sqrt(s + eps)

    def _ln_t(v, eps=1e-5):
        m = jnp.mean(v, axis=-1, keepdims=True)
        s = jnp.var(v, axis=-1, keepdims=True)
        return (v - m) / jnp.sqrt(s + eps)

    def _to_tokens(v):
        B_, C_, H_, W_ = v.shape
        return v.reshape(B_, C_, H_ * W_).transpose(0, 2, 1)
    def _from_tokens(t, like):
        B_, C_, H_, W_ = like.shape
        return t.transpose(0, 2, 1).reshape(B_, C_, H_, W_)

    x = x + _L0_conv_ref(_gn(x), L0_conv_f_in_w, L0_conv_f_conv_w, L0_conv_f_conv_b, L0_conv_f_xproj_w, L0_conv_f_dt_w, L0_conv_f_dt_b, L0_conv_f_Alog, L0_conv_f_D, L0_conv_f_out_w, L0_conv_b_in_w, L0_conv_b_conv_w, L0_conv_b_conv_b, L0_conv_b_xproj_w, L0_conv_b_dt_w, L0_conv_b_dt_b, L0_conv_b_Alog, L0_conv_b_D, L0_conv_b_out_w, L0_conv_fuse_w, L0_conv_ln_w, L0_conv_ln_b)
    t = _to_tokens(x)
    t = t + _L1_attn_ref(_ln_t(t), L1_attn_W1, L1_attn_b1, L1_attn_w2, L1_attn_b2)
    t = t + _L1_ffn_ref(_ln_t(t), L1_ffn_router_w, L1_ffn_router_b, L1_ffn_expert_w, L1_ffn_expert_b)
    x = _from_tokens(t, x)
    return x


_drawn_inputs = setup_inputs


def setup_inputs(seed=0):
    import zlib

    import numpy as np

    out = dict(_drawn_inputs(seed))
    spreads = {'L0_conv_ln_w': (1.0, 0.2),
     'L0_conv_ln_b': (0.0, 0.1),
     'L1_ffn_router_b': (0.0, 0.1),
     'L1_ffn_expert_b': (0.0, 0.1)}
    factors = {'L0_conv_f_dt_w': 31.486,
     'L0_conv_f_dt_b': 5.849,
     'L0_conv_f_Alog': 15.601,
     'L0_conv_b_dt_w': 33.483,
     'L0_conv_b_dt_b': 6.353,
     'L0_conv_b_Alog': 18.276,
     'L1_attn_b1': 5.171}
    for name, (base, spread) in spreads.items():
        noise = np.random.default_rng([zlib.crc32(name.encode()), seed]).standard_normal(out[name].shape)
        drawn = base * np.exp(spread * noise) if base else spread * noise
        out[name] = jnp.asarray(drawn.astype(out[name].dtype))
    for name, factor in factors.items():
        out[name] = (out[name] * factor).astype(out[name].dtype)
    return out
```

```python
from contextlib import ExitStack

import concourse.bass as bass
from concourse import mybir

F32 = mybir.dt.float32
BF16 = mybir.dt.bfloat16
ALU = mybir.AluOpType
ACT = mybir.ActivationFunctionType
AX = mybir.AxisListType

P = 128
DIRS = 2
STATE = 16
TAPS = 4
RANK = 8
EXPERTS = 8
HEADS = 16
IB = P // HEADS
BANK = 512


def hybrid_kernel(nc, x, in_wT, conv_wT, conv_b, xproj_w, xprojT, dt_wT, dt_b, Alog, Dp, out_w, fuseT,
                  ln_w, ln_b, W1, b1t, w2t, b2, router_w, router_b, expert_w, expert_b, out):
    NM, C, T, V = x.shape
    TOK = T * V
    NT = TOK // P
    H2 = in_wT.shape[2] // (2 * P)
    SEQ = [22, 21, 21]
    CH = len(SEQ)
    S0 = [sum(SEQ[:c]) for c in range(CH)]
    CW = SEQ[0] * V
    BC = 2 * STATE
    B_AHEAD = 3
    NBS = 3
    TAIL = 4
    PART = 32
    PW = BANK
    STEPS = CH * STATE
    TC = [(k, min(k + BANK, TOK)) for k in range(0, TOK, BANK)]
    NB = TOK // IB
    assert C == P and sum(SEQ) == T and CW <= BANK and TOK % P == 0

    ctx = ExitStack()
    with ctx:
        def sb(name, shape, dt=F32):
            return ctx.enter_context(nc.sbuf_tensor(name, shape, dt))

        def sem(name):
            return ctx.enter_context(nc.semaphore(name))

        w_z = sb("w_z", [P, DIRS, 2 * P])
        w_conv = sb("w_conv", [P, DIRS, TAPS, 2 * P])
        w_bc = sb("w_bc", [P, DIRS, H2, 3 * BC])
        w_dt = sb("w_dt", [P, DIRS, H2, 2 * P])
        w_fo = sb("w_fo", [P, DIRS, H2, P])
        cb = sb("cb", [P, DIRS, H2])
        cbh = sb("cbh", [P, DIRS, H2])
        dtb = sb("dtb", [P, DIRS, H2])
        dD = sb("dD", [P, DIRS, H2])
        aneg = sb("aneg", [P, DIRS, H2, STATE])
        lnw = sb("lnw", [P, 1])
        lnb = sb("lnb", [P, 1])
        w1 = sb("w1", [P, 2, HEADS])
        w1r = sb("w1r", [P, 2, IB, HEADS])
        b1c = sb("b1c", [P, 1])
        w2c = sb("w2c", [P, 1])
        b2c = sb("b2c", [P, 1])
        rw = sb("rw", [P, EXPERTS])
        rb = sb("rb", [P, EXPERTS])
        ew = sb("ew", [P, EXPERTS, P])
        eb = sb("eb", [3 * PART, P])
        ident = sb("ident", [P, P])
        gavg = sb("gavg", [P, P])
        pick = sb("pick", [3 * BC, BC, P], BF16)
        mask8 = sb("mask8", [P, IB])
        below = sb("below", [P, P])
        earlier = sb("earlier", [P, EXPERTS, EXPERTS])
        w2b = sb("w2b", [P, 4, 32])
        zero = sb("zero", [P, P], BF16)
        mhalf = sb("mhalf", [P, NT])

        X = sb("X", [P, TOK])
        PAD = TAPS - 1
        XP = sb("XP", [P, T, V + 2 * PAD])
        M = sb("M", [P, 8, TOK])
        W = sb("W", [P, 4, TOK])
        G = sb("G", [P, 4, TOK])
        S3 = sb("S3", [3 * BC, TOK], BF16)
        Bs = sb("Bs", [P, NBS, CW])
        DA = sb("DA", [P, 2, 2 * CW])
        DBU = sb("DBU", [P, 2, 2 * CW])
        HS = sb("HS", [P, 2, 2 * CW])
        HC = sb("HC", [P, 2, 2 * CW])
        YT = sb("YT", [P, 2, CW])
        T12 = sb("T12", [P, TOK])
        XH = sb("XH", [P, NT, P + 1])
        GR = sb("GR", [P, TOK])
        EX = sb("EX", [P, 2, PW])
        ET = sb("ET", [P, TOK])
        FC = sb("FC", [P, NB])
        st = sb("st", [P, 4, NT, 6])
        mv = sb("mv", [P, 4, NT, 2])
        va = sb("va", [P, 3, NT])
        rs = sb("rs", [P, 3, NT])
        gm = sb("gm", [P, 2])
        gsm = sb("gsm", [P, 4])
        rc = sb("rc", [P, 2])

        XC, ZS, DT, DU = (M[:, 2 * i:2 * i + 2, :] for i in range(4))
        THS = [W[:, :, :].rearrange("p a n -> p (a n)")[:, i * PW:(i + 1) * PW] for i in range(4 * TOK // PW)]
        RING = len(THS)
        BCF = W[0:3 * BC, 0, :]
        S3m = W[0:3 * BC, 1, 0:TOK // 2].bitcast(BF16)
        YN, XHT, FT = (W[:, i, :] for i in range(3))
        PX = W[:, 3, 0:NT * 3 * PART].rearrange("p (t e) -> p t e", t=NT)
        X3, X3T, XL, T2C = (M[:, i, :] for i in range(4))
        OUT = X3
        PT = M[0:3 * PART, 4, :]
        PTB = M[0:3 * PART, 5, 0:TOK // 2].bitcast(BF16)
        XG = M[:, 6, 0:2 * BANK].rearrange("p (a n) -> p a n", a=2)
        NE = NT * EXPERTS
        LG, LP = (M[:, 6, 2 * BANK + i * NE:2 * BANK + (i + 1) * NE].rearrange("p (t e) -> p t e", t=NT) for i in range(2))
        RK = M[:, 6, 2 * BANK + 2 * NE:2 * BANK + 3 * NE]
        LB = M[:, 6, 2 * BANK + 3 * NE:2 * BANK + 3 * NE + NE // 2].bitcast(BF16).rearrange("p (t e) -> p t e", t=NT)
        MX = M[:, 6, 2 * BANK + 4 * NE:2 * BANK + 4 * NE + NT]
        CMP, CMQ = (M[:, 7, i * NT * EXPERTS * EXPERTS:(i + 1) * NT * EXPERTS * EXPERTS]
                    .rearrange("p (t e) -> p t e", e=EXPERTS) for i in range(2))
        taps = W[:, 0:DIRS, 0:TAPS * 2 * P]
        w_out = W[:, 2, 0:DIRS * 2 * P].rearrange("p (d n) -> p d n", d=DIRS)
        w_fuse = W[:, 2, DIRS * 2 * P:DIRS * 3 * P].rearrange("p (d n) -> p d n", d=DIRS)
        w_xr, w_dr = (W[0:RANK, 3, i * DIRS * 2 * P:(i + 1) * DIRS * 2 * P].rearrange("p (d n) -> p d n", d=DIRS)
                      for i in range(2))
        w_xp = M[:, 0, 0:DIRS * H2 * (RANK + BC)].rearrange("p (d h n) -> p d h n", d=DIRS, h=H2)
        w_in = M[:, 1, 0:DIRS * 4 * P // 2].rearrange("p (d n) -> p d n", d=DIRS)

        ps = ctx.enter_context(nc.psum_tensor("ps", [P, 8, BANK], F32))
        B_BANK, C_BANK, Y_BANK, S_BANK, A_BANK = 0, 1, 3, 5, 7
        WORK = 5

        s_set = sem("s_set")
        s_dve0 = sem("s_dve0")
        s_pool0 = sem("s_pool0")
        s_act0 = sem("s_act0")
        s_pe0 = sem("s_pe0")

        per_sample = ("s_x v_link a_link gn_stats gn_avg gn_var gn_rstd xn_ready xb_ready proj_ps hu_ev "
                      "th_ready silu_done bc_ps bc_ev s3_ready dt_ps x_ready tm_ready sp_ready dt_done du_ready "
                      "b_bc b_ev da_ready dbu_done scan_done c_bc hc_done y_sum y_fin g_done "
                      "o_ps var_y rstd_y yn_ready yt_ps x1_ready xt_ps t1_ev var_t rstd_t xh_ready xht_ps xht_ev fr_ps "
                      "fc_part fc_ready gr_ps gr_ev th_att sc_mm exp_done mask_done et_tr et_ev oo_done t2_done t2_copy "
                      "var_x rstd_x x3_ready x3t_ps x3t_ev lg_ps lg_ready pexp px_zero pg_ready pt_ps pt_ev e_bc xg_done "
                      "e_mm out_ready s_out").split()
        sm = {name: sem(name) for name in per_sample}
        (s_x, v_link, a_link, gn_stats, gn_avg, gn_var, gn_rstd, xn_ready, xb_ready, proj_ps, hu_ev,
         th_ready, silu_done, bc_ps, bc_ev, s3_ready, dt_ps, x_ready, tm_ready, sp_ready, dt_done, du_ready,
         b_bc, b_ev, da_ready, dbu_done, scan_done, c_bc, hc_done, y_sum, y_fin, g_done,
         o_ps, var_y, rstd_y, yn_ready, yt_ps, x1_ready, xt_ps, t1_ev, var_t, rstd_t, xh_ready, xht_ps, xht_ev, fr_ps,
         fc_part, fc_ready, gr_ps, gr_ev, th_att, sc_mm, exp_done, mask_done, et_tr, et_ev, oo_done, t2_done, t2_copy,
         var_x, rstd_x, x3_ready, x3t_ps, x3t_ev, lg_ps, lg_ready, pexp, px_zero, pg_ready, pt_ps, pt_ev, e_bc, xg_done,
         e_mm, out_ready, s_out) = (sm[name] for name in per_sample)
        nums = sorted(s.num for s in sm.values())
        assert nums == list(range(nums[0], nums[-1] + 1))

        def chunk(c):
            return slice(S0[c] * V, (S0[c] + SEQ[c]) * V)

        def seqs(c):
            return slice(S0[c], S0[c] + SEQ[c])

        loads = [
            (w_in, in_wT[:, :, 0:2 * P].rearrange("d p n -> p d n")),
            (w_z[:, :, :], in_wT[:, :, 2 * P:].rearrange("d p n -> p d n")),
            (w_xp, xprojT.rearrange("d (h p) n -> p d h n", p=P)),
            (w_xr[:, :, :], xproj_w[:, 0:RANK, :].rearrange("d r n -> r d n")),
            (w_dr[:, :, :], dt_wT.rearrange("d r n -> r d n")),
            (w_out[:, :, :], out_w.rearrange("d p n -> p d n")),
            (w_fuse[:, :, :], fuseT.rearrange("(d p) n -> p d n", p=P)),
            (cb[:, :, :], conv_b.rearrange("d (h p) -> p d h", p=P)),
            (dtb[:, :, :], dt_b.rearrange("d (h p) -> p d h", p=P)),
            (dD[:, :, :], Dp.rearrange("d (h p) -> p d h", p=P)),
            (aneg[:, :, :, :], Alog.rearrange("d (h p) s -> p d h s", p=P)),
            (lnw[:, :], ln_w.rearrange("(p a) -> p a", a=1)),
            (lnb[:, :], ln_b.rearrange("(p a) -> p a", a=1)),
            (w1[:, :, :], W1.rearrange("(g p) a -> p g a", p=P)),
            (b1c[:, :], b1t.rearrange("(p a) -> p a", a=1)),
            (w2c[:, :], w2t.rearrange("(p a) -> p a", a=1)),
            (b2c[:, :], b2.partition_broadcast(P)),
            (rw[:, :], router_w),
            (rb[:, :], router_b.partition_broadcast(P)),
            (ew[:, :, :], expert_w.rearrange("e p n -> p e n")),
        ] + [(eb[PART * i:PART * i + EXPERTS, :], expert_b) for i in range(3)
        ] + [(taps[:, d, :], conv_wT[d].partition_broadcast(P)) for d in range(DIRS)]

        with nc.Block() as block:
            @block.sync
            def _(sp):
                sp.wait_ge(s_dve0, 1)
                with nc.allow_non_contiguous_dma(reason="small parameters, once"):
                    for dst, src in loads:
                        sp.dma_start(dst, src).then_inc(s_set, 16)

            @block.gpsimd
            def _(pool):
                n = 0
                for t, value in ((ident, 0.0), (gavg, 0.25), (pick, 0.0), (mask8, 1.0), (below, 1.0),
                                 (earlier, 1.0), (w2b, 0.0), (zero, 0.0), (mhalf, -0.5)):
                    pool.memset(t[...], value).then_inc(s_pool0, 1)
                    n += 1
                pool.wait_ge(s_pool0, n)

                def select(ap, op, fill, base, pattern, mult):
                    nonlocal n
                    pool.affine_select(out=ap, in_=ap, compare_op=op, fill=fill, base=base, pattern=pattern,
                                       channel_multiplier=mult).then_inc(s_pool0, 1)
                    n += 1
                    pool.wait_ge(s_pool0, n)

                select(ident[:, :], ALU.not_equal, 1.0, 0, [[-1, P]], 1)
                select(gavg[:, :], ALU.is_ge, 0.0, 0, [[-4, P // 4], [0, 4]], 1)
                select(gavg[:, :], ALU.is_ge, 0.0, 3, [[4, P // 4], [0, 4]], -1)
                for q in range(3):
                    select(pick[:, :, :], ALU.not_equal, 1.0, -BC * q, [[-1, BC], [0, P]], 1)
                select(mask8[:, :], ALU.is_ge, 0.0, 0, [[-HEADS, IB]], 1)
                select(mask8[:, :], ALU.is_ge, 0.0, HEADS - 1, [[HEADS, IB]], -1)
                select(below[:, :], ALU.is_ge, 0.0, -1, [[-1, P]], 1)
                select(earlier[:, :, :], ALU.is_ge, 0.0, -1, [[1, EXPERTS], [-1, EXPERTS]], 0)
                pool.memset(XP[:, :, :], 0.0).then_inc(s_pool0, 1)
                pool.memset(DA[:, :, :], 0.0).then_inc(s_pool0, 1)
                pool.memset(XH[:, :, :], 1.0).then_inc(s_pool0, 1)
                n += 3
                pool.wait_ge(s_pool0, n)
                assert n == 22

            @block.scalar
            def _(act):
                act.wait_ge(s_set, 16 * len(loads))
                act.activation(aneg[...], aneg[...], ACT.Exp).then_inc(s_act0, 1)

            @block.tensor
            def _(pe):
                pe.wait_ge(s_set, 16 * len(loads))
                for d in range(DIRS):
                    for k in range(H2):
                        pe.matmul(ps[:, 2 * d + k, 0:2 * P], w_xr[:, d, k * P:(k + 1) * P], w_dr[:, d, :],
                                  start=True, stop=True)
                        last = pe.matmul(ps[:, 4 + 2 * d + k, 0:P], w_out[:, d, k * P:(k + 1) * P], w_fuse[:, d, :],
                                         start=True, stop=True)
                last.then_inc(s_pe0, 1)

            @block.vector
            def _(dve):
                dve.memset(eb[:, :], 0.0).then_inc(s_dve0, 1)
                dve.wait_ge(s_set, 16 * len(loads))
                dve.wait_ge(s_pool0, 22)
                for d in range(DIRS):
                    dve.tensor_tensor(w_conv[:, d, :, :],
                                      w_in[:, d, 0:2 * P].unsqueeze(1).broadcast_to([P, TAPS, 2 * P]),
                                      taps[:, d, :].rearrange("p (k n) -> p k n", k=TAPS), ALU.mult).then_inc(s_dve0, 1)
                    for k in range(H2):
                        dve.tensor_copy(w_bc[:, d, k, :].rearrange("p (q n) -> p q n", q=3),
                                        w_xp[:, d, k, RANK:].unsqueeze(1).broadcast_to([P, 3, BC])).then_inc(s_dve0, 1)
                dve.tensor_scalar(cbh[...], cb[...], 0.5, None, ALU.mult).then_inc(s_dve0, 1)
                for g in range(2):
                    dve.tensor_copy(w1r[:, g, :, :],
                                    w1[:, g, :].unsqueeze(1).broadcast_to([P, IB, HEADS])).then_inc(s_dve0, 1)
                for r in range(4):
                    dve.tensor_scalar(w2b[:, r, IB * r:IB * r + IB], mask8[:, :], w2c[:, 0:1], None,
                                      ALU.mult).then_inc(s_dve0, 1)
                dve.wait_ge(s_act0, 1)
                dve.tensor_scalar(aneg[...], aneg[...], -1.0, None, ALU.mult).then_inc(s_dve0, 1)
                dve.wait_ge(s_pe0, 1)
                for d in range(DIRS):
                    for k in range(H2):
                        dve.tensor_copy(w_dt[:, d, k, :], ps[:, 2 * d + k, 0:2 * P]).then_inc(s_dve0, 1)
                        dve.tensor_copy(w_fo[:, d, k, :], ps[:, 4 + 2 * d + k, 0:P]).then_inc(s_dve0, 1)
                dve.wait_ge(s_dve0, 1 + DIRS * (1 + H2) + 1 + 2 + 4 + 1 + 2 * DIRS * H2)

        nc.all_engine_barrier()

        passes = []
        for it in range(NT):
            parts = (P * (it + 1) + PW - 1) // PW
            cuts = [P * ((it + 1) * i // parts) for i in range(parts + 1)]
            passes += [(it, cuts[i], cuts[i + 1]) for i in range(parts)]
        NP = len(passes)

        def width(p, q):
            it, a, b = passes[p]
            return min(b, P * it + 32 * (q + 1)) - a

        def place_attention(parts):
            def time(p, q):
                return 0.186 + width(p, q) * 0.00083

            total = sum(parts)
            left = sum(4 * time(p, q) for p in range(NP) for q in range(4))
            last = [sum(parts[:i + 1]) - 2 for i in range(len(parts) - 1)]
            plan = [[] for _ in range(3 * total)]
            scored, turned, units = {}, {}, [(p, r) for p in range(NP) for r in range(4)]
            u = q = j = chain = 0
            budget = 0.0
            exp_at = {-2: -1, -1: -1}
            while u < len(units):
                rate = max(left / max(total - TAIL - j - sum(j <= x for x in last), 1), 1.2)
                budget = min(budget + rate, 1.3 * rate)
                while u < len(units) and (budget > 0 or j in last and q > 0):
                    p, r = units[u]
                    t = 4 * u + q
                    if t >= RING and scored.get((t - RING) // 4, j) >= j:
                        break
                    if q == 0 and any(x <= j < x + 2 for x in last):
                        break
                    plan[j].append(("tanh", p, r, q))
                    budget -= time(p, q)
                    left -= time(p, q)
                    q += 1
                    if q < 4:
                        continue
                    at = max(j + 1, exp_at[p - 2] + 1, scored.get(u - 1, 0))
                    plan[at].append(("score", p, r))
                    scored[u] = at
                    q, u = 0, u + 1
                    if r == 3:
                        e = max(at + 1, turned.get(p - 2, -1) + 1)
                        plan[e].append(("exp", p))
                        plan[e + 1].append(("mask", p))
                        exp_at[p] = e
                        chain = max(chain, e + 2)
                        plan[chain].append(("turn", p))
                        plan[chain + 1].append(("fetch", p))
                        turned[p] = chain
                        chain += 2
                        it, _, b = passes[p]
                        if b == P * (it + 1):
                            plan[chain].append(("sum", it))
                            plan[chain + 1].append(("scale", it))
                            chain += 2
                j += 1
            while not plan[-1]:
                plan.pop()
            return plan

        def body(n, mamba, attn):
            plan = place_attention([STEPS + 1, STEPS + 1] if mamba else [120]) if attn else []
            if mamba:
                by_step = [plan[i] if i < len(plan) else [] for i in range(2 * (STEPS + 1))]
                rest = plan[2 * (STEPS + 1):]
            else:
                by_step, rest = [], plan

            def chain_end(emit):
                for items in rest:
                    for item in items:
                        emit(item)

            with nc.Block() as block:
                @block.sync
                def _(sp):
                    if mamba:
                        sp.wait_ge(g_done, DIRS * CH * H2)
                        m = (n + 1) % NM
                        sp.dma_start(XL, x[bass.ds(m, 1)].rearrange("a p t v -> p (a t v)")).then_inc(s_x, 16)
                    if attn:
                        for i, (a, b) in enumerate(TC):
                            sp.wait_ge(out_ready, i + 1)
                            sp.dma_start(out[bass.ds(n - 1, 1)].rearrange("a p t v -> p (a t v)")[:, a:b],
                                         OUT[:, a:b]).then_inc(s_out, 16)
                        sp.wait_ge(s_out, 16 * len(TC))

                @block.gpsimd
                def _(pool):
                    def rstd(i, ready, done):
                        pool.wait_ge(ready, 1)
                        pool.tensor_tensor(rs[:, i, :], va[:, i, :], mhalf[:, :], ALU.pow).then_inc(done, 1)

                    def gate(q):
                        d, c = divmod(q, CH)
                        for h in range(H2):
                            pool.wait_ge(y_fin, H2 * q + h + 1)
                            g = G[:, 2 * d + h, chunk(c)]
                            if d == 1:
                                g = g.rearrange("p (s v) -> p s v", v=V)[:, :, ::-1]
                                a = YT[:, h, 0:SEQ[c] * V].rearrange("p (s v) -> p s v", v=V)
                                b = ZS[:, h, chunk(c)].rearrange("p (s v) -> p s v", v=V)
                            else:
                                a, b = YT[:, h, 0:SEQ[c] * V], ZS[:, h, chunk(c)]
                            pool.tensor_tensor(g, a, b, ALU.mult).then_inc(g_done, 1)

                    def attend(item):
                        if item[0] == "mask":
                            p = item[1]
                            it, a, b = passes[p]
                            pool.wait_ge(exp_done, p + 1)
                            if b == P * (it + 1):
                                e = EX[:, p % 2, it * P - a:b - a]
                                pool.tensor_tensor(e, e, below[:, :], ALU.mult).then_inc(mask_done, 1)

                    if mamba:
                        for d in range(DIRS):
                            for h in range(H2):
                                pool.wait_ge(dt_done, H2 * d + h + 1)
                                pool.wait_ge(silu_done, 4 * d + 4)
                                pool.tensor_tensor(DU[:, h, :], DT[:, h, :], XC[:, h, :], ALU.mult).then_inc(du_ready, 1)
                            pool.wait_ge(du_ready, H2 * (d + 1))
                            for k in range(STEPS + 1):
                                if k < STEPS:
                                    K = STEPS * d + k
                                    c = k // STATE
                                    w = SEQ[c] * V
                                    pool.wait_ge(b_ev, K + 1)
                                    if K >= 2:
                                        pool.wait_ge(scan_done, K - 1)
                                    pool.tensor_tensor(DBU[:, K % 2, 0:2 * w].rearrange("p (h n) -> p h n", h=2),
                                                       DU[:, :, chunk(c)],
                                                       Bs[:, K % NBS, 0:w].unsqueeze(1).broadcast_to([P, 2, w]),
                                                       ALU.mult).then_inc(dbu_done, 1)
                                for item in by_step[d * (STEPS + 1) + k]:
                                    attend(item)
                                if k % STATE == 4 and k > STATE:
                                    gate(CH * d + k // STATE - 1)
                            gate(CH * d + CH - 1)
                    chain_end(attend)
                    if attn:
                        pool.memset(PX[...], 0.0).then_inc(px_zero, 1)
                        pool.wait_ge(t2_done, NT)
                        if mamba:
                            pool.wait_ge(y_fin, DIRS * CH * H2)
                            pool.wait_ge(g_done, DIRS * CH * H2)
                        pool.tensor_copy(T2C[...], T12[:, :]).then_inc(t2_copy, 1)
                        rstd(0, var_x, rstd_x)
                    if mamba:
                        rstd(1, var_y, rstd_y)
                        pool.wait_ge(gn_var, 1)
                        pool.tensor_tensor(gsm[:, 3:4], gsm[:, 2:3], mhalf[:, 0:1], ALU.pow).then_inc(gn_rstd, 1)
                        rstd(2, var_t, rstd_t)
                        pool.wait_ge(s_x, 16)
                        pool.wait_ge(xt_ps, len(TC))
                        pool.tensor_scalar(X[:, :], XL, lnb[:, 0:1], None, ALU.add).then_inc(xb_ready, 1)

                @block.scalar
                def _(act):
                    def attend(item):
                        if item[0] == "tanh":
                            _, p, r, q = item
                            t = 4 * (4 * p + r) + q
                            if t >= RING:
                                act.wait_ge(sc_mm, t - RING + 1)
                            it, a, b = passes[p]
                            L = width(p, q)
                            act.activation(THS[t % RING][:, 0:L], GR[:, a:a + L], ACT.Tanh,
                                           bias=FC[:, 16 * it + 4 * q + r:16 * it + 4 * q + r + 1]).then_inc(th_att, 1)
                        if item[0] == "exp":
                            p = item[1]
                            it, a, b = passes[p]
                            act.wait_ge(sc_mm, 16 * (p + 1))
                            if p >= 2:
                                act.wait_ge(et_tr, p - 1)
                            act.activation(EX[:, p % 2, 0:b - a], ps[:, S_BANK + p % 2, 0:b - a], ACT.Exp, bias=b2c[:, 0:1]).then_inc(exp_done, 1)

                    if mamba:
                        for d in range(DIRS):
                            if d == 1 and attn:
                                act.wait_ge(sc_mm, 4 * sum(i[0] == "score" for s in by_step[:STEPS + 1] for i in s))
                            for u in range(4):
                                if 4 * d + u >= 2:
                                    act.wait_ge(silu_done, 4 * d + u - 1)
                                if d == 1 and u == 0:
                                    act.wait_ge(dt_done, H2)
                                for c in range(CH):
                                    j = CH * u + c
                                    act.wait_ge(proj_ps, 4 * CH * d + j + 1)
                                    src, dst = ps[:, j % WORK, 0:SEQ[c] * V], W[:, u % 2, chunk(c)]
                                    if u < 2:
                                        act.activation(dst, src, ACT.Identity, bias=cbh[:, d, u:u + 1],
                                                       scale=0.5).then_inc(hu_ev, 1)
                                    else:
                                        act.activation(dst, src, ACT.Copy, scale=0.5).then_inc(hu_ev, 1)
                                act.wait_ge(hu_ev, 4 * CH * d + CH * (u + 1))
                                act.activation(W[:, 2 + u % 2, :], W[:, u % 2, :], ACT.Tanh).then_inc(th_ready, 1)
                            for c in range(CH):
                                act.wait_ge(bc_ps, CH * d + c + 1)
                                if c == 0:
                                    act.wait_ge(silu_done, 4 * d + 4)
                                    if d == 1:
                                        act.wait_ge(c_bc, STEPS)
                                src = ps[0:3 * BC, (4 * CH + c) % WORK, 0:SEQ[c] * V]
                                act.activation(S3[:, chunk(c)], src, ACT.Copy).then_inc(bc_ev, 1)
                                act.activation(BCF[:, chunk(c)], src, ACT.Copy).then_inc(bc_ev, 1)
                            for h in range(H2):
                                act.wait_ge(tm_ready, H2 * d + h + 1)
                                act.activation(W[:, 2 + h, :], W[:, 2 + h, :], ACT.Exp).then_inc(a_link, 1)
                            for h in range(H2):
                                act.wait_ge(a_link, H2 * d + h + 1)
                                act.activation(W[:, 2 + h, :], W[:, 2 + h, :], ACT.Ln, bias=1.0).then_inc(sp_ready, 1)
                            act.wait_ge(dt_done, H2 * (d + 1))
                            for k in range(STEPS + 1):
                                if k < STEPS:
                                    K = STEPS * d + k
                                    c, s = divmod(k, STATE)
                                    w = SEQ[c] * V
                                    if K >= 2:
                                        act.wait_ge(scan_done, K - 1)
                                    for h in range(H2):
                                        act.activation(
                                            DA[:, K % 2, h * w:(h + 1) * w].rearrange("p (s v) -> p s v", v=V)[:, :, 1:V],
                                            DT[:, h, chunk(c)].rearrange("p (s v) -> p s v", v=V)[:, :, 1:V],
                                            ACT.Exp, scale=aneg[:, d, h, s:s + 1]).then_inc(da_ready, 1)
                                if k == 0 and attn:
                                    act.wait_ge(s3_ready, 2 * (d + 1))
                                for item in by_step[d * (STEPS + 1) + k]:
                                    attend(item)
                    chain_end(attend)

                    def copy_out(dst, bank, ready, done):
                        for i, (a, b) in enumerate(TC):
                            act.wait_ge(ready, i + 1)
                            act.activation(dst[:, a:b], ps[:, bank + i, 0:b - a], ACT.Copy).then_inc(done, 1)

                    if attn:
                        act.wait_ge(t2_done, NT)
                        if mamba:
                            act.wait_ge(g_done, DIRS * CH * H2)
                        copy_out(X3T, 3, x3t_ps, x3t_ev)
                        act.wait_ge(lg_ready, 1)
                        act.activation(LP[...], LP[...], ACT.Exp).then_inc(pexp, 1)
                    if mamba:
                        if attn:
                            act.wait_ge(t2_copy, 1)
                            act.wait_ge(x3_ready, NT)
                        copy_out(T12, 3, xt_ps, t1_ev)
                    if attn:
                        for i, (a, b) in enumerate(TC):
                            act.wait_ge(pt_ps, i + 1)
                            act.activation(PTB[:, a:b], ps[0:3 * PART, i, 0:b - a], ACT.Copy).then_inc(pt_ev, 1)
                            act.activation(PT[:, a:b], ps[0:3 * PART, i, 0:b - a], ACT.Copy).then_inc(pt_ev, 1)
                    if mamba:
                        copy_out(XHT, 3, xht_ps, xht_ev)
                    for part in range(len(TC)):
                        if mamba and part == 2:
                            copy_out(GR, 3, gr_ps, gr_ev)
                        if attn:
                            a, b = TC[part]
                            act.wait_ge(e_mm, EXPERTS * (part + 1))
                            act.activation(OUT[:, a:b], ps[:, part, 0:b - a], ACT.Copy).then_inc(out_ready, 1)

                @block.tensor
                def _(pe):
                    def attend(item):
                        if item[0] == "score":
                            _, p, r = item
                            it, a, b = passes[p]
                            S = S_BANK + p % 2
                            if r == 0:
                                if p >= 2:
                                    pe.wait_ge(exp_done, p - 1)
                                if b == P * (it + 1):
                                    pe.matmul(ps[:, S, P * it - a:b - a], zero[:, :], zero[:, :],
                                              start=True, stop=True, skip_group_check=True)
                            t = 4 * (4 * p + r)
                            pe.wait_ge(th_att, t + 4)
                            for q in range(4):
                                L = width(p, q)
                                pe.matmul(ps[32 * q:32 * q + 32, S, 0:L], w2b[:, r, :], THS[(t + q) % RING][:, 0:L],
                                          start=(r == 0), stop=(r == 3), skip_group_check=True).then_inc(sc_mm, 1)
                        if item[0] == "turn":
                            p = item[1]
                            it, a, b = passes[p]
                            pe.wait_ge(mask_done, sum(y == P * (i + 1) for i, _, y in passes[:p + 1]))
                            pe.wait_ge(exp_done, p + 1)
                            if p >= 1:
                                pe.wait_ge(et_ev, p)
                            if it >= 1:
                                pe.wait_ge(t2_done, it)
                            for o in range(0, b - a, P):
                                last = pe.transpose(ps[:, A_BANK, o:o + P], EX[:, p % 2, o:o + P], ident[:, :])
                            last.then_inc(et_tr, 1)
                        if item[0] == "sum":
                            it = item[1]
                            pe.wait_ge(et_ev, sum(i <= it for i, _, _ in passes))
                            for jt in range(it + 1):
                                last = pe.matmul(ps[:, A_BANK, 0:P + 1], ET[:, jt * P:(jt + 1) * P], XH[:, jt, :],
                                                 start=(jt == 0), stop=(jt == it))
                            last.then_inc(oo_done, 1)

                    def taken(d, c, t):
                        if d == 0:
                            return XP[:, seqs(c), t:t + V]
                        last = V + 2 * PAD - 1 - t
                        return XP[:, seqs(c), last:last - V:-1]

                    def project(d):
                        if d == 1:
                            pe.wait_ge(y_fin, H2 * CH)
                            pe.wait_ge(b_ev, STEPS)

                        def bank(j):
                            i = j - WORK
                            if 0 <= i < 4 * CH:
                                pe.wait_ge(hu_ev, 4 * CH * d + i + 1)
                            elif 4 * CH <= i < 5 * CH:
                                pe.wait_ge(bc_ev, 2 * (CH * d + i - 4 * CH + 1))
                            elif i >= 5 * CH:
                                pe.wait_ge(x_ready, H2 * CH * d + i - 5 * CH + 1)
                            return j % WORK

                        for u in range(4):
                            for c in range(CH):
                                o = ps[:, bank(CH * u + c), 0:SEQ[c] * V]
                                if u < 2:
                                    for t in range(TAPS):
                                        last = pe.matmul(o, w_conv[:, d, t, u * P:(u + 1) * P],
                                                         taken(d, c, t),
                                                         start=(t == 0), stop=(t == TAPS - 1))
                                else:
                                    last = pe.matmul(o, w_z[:, d, (u - 2) * P:(u - 1) * P], taken(d, c, PAD),
                                                     start=True, stop=True)
                                last.then_inc(proj_ps, 1)
                        pe.wait_ge(silu_done, 4 * d + 2)
                        for c in range(CH):
                            j = bank(4 * CH + c)
                            for k in range(H2):
                                last = pe.matmul(ps[0:3 * BC, j, 0:SEQ[c] * V], w_bc[:, d, k, :], XC[:, k, chunk(c)],
                                                 start=(k == 0), stop=(k == H2 - 1))
                            last.then_inc(bc_ps, 1)
                        for h in range(H2):
                            for c in range(CH):
                                j = bank(5 * CH + CH * h + c)
                                for k in range(H2):
                                    last = pe.matmul(ps[:, j, 0:SEQ[c] * V], w_dt[:, d, k, h * P:(h + 1) * P],
                                                     XC[:, k, chunk(c)], start=(k == 0), stop=(k == H2 - 1))
                                last.then_inc(dt_ps, 1)

                    def spread_b(K):
                        d, k = divmod(K, STEPS)
                        c, s = divmod(k, STATE)
                        w = SEQ[c] * V
                        if K >= 1:
                            pe.wait_ge(b_ev, K)
                        pe.matmul(ps[:, B_BANK, 0:w], pick[:, s, :], S3[:, chunk(c)], start=True, stop=True).then_inc(b_bc, 1)

                    def spread_c(K):
                        d, k = divmod(K, STEPS)
                        c, s = divmod(k, STATE)
                        w = SEQ[c] * V
                        if K >= 2:
                            pe.wait_ge(hc_done, K - 1)
                        pe.matmul(ps[:, C_BANK + K % 2, 0:w], pick[:, STATE + s, :], S3[:, chunk(c)],
                                  start=True, stop=True).then_inc(c_bc, 1)

                    def add_up(K):
                        d, k = divmod(K, STEPS)
                        c, s = divmod(k, STATE)
                        q = CH * d + c
                        w = SEQ[c] * V
                        if s == 0 and q >= 1:
                            pe.wait_ge(y_fin, H2 * q)
                        pe.wait_ge(hc_done, K + 1)
                        for h in range(H2):
                            last = pe.matmul(ps[:, Y_BANK + h, 0:w], ident[:, :], HC[:, K % 2, h * w:(h + 1) * w],
                                             start=(s == 0), stop=(s == STATE - 1))
                        last.then_inc(y_sum, 1)

                    if mamba:
                        for d in range(DIRS):
                            project(d)
                            pe.wait_ge(s3_ready, 2 * (d + 1))
                            pe.wait_ge(x_ready, H2 * CH * (d + 1))
                            for k in range(-B_AHEAD, STEPS + 2):
                                if k + B_AHEAD < STEPS:
                                    spread_b(STEPS * d + k + B_AHEAD)
                                if 0 <= k < STEPS:
                                    spread_c(STEPS * d + k)
                                if k >= 2:
                                    add_up(STEPS * d + k - 2)
                                if 0 <= k <= STEPS:
                                    for item in by_step[d * (STEPS + 1) + k]:
                                        attend(item)
                    chain_end(attend)

                    def turn(src, bank, rows, free, done):
                        for t in range(NT):
                            free(t)
                            i = pe.transpose(ps[0:rows, bank + t // 4, P * (t % 4):P * (t % 4) + P], src(t), ident[:, :])
                            if t % 4 == 3 or t == NT - 1:
                                i.then_inc(done, 1)

                    if mamba:
                        pe.wait_ge(g_done, DIRS * CH * H2)
                        pe.wait_ge(b_ev, DIRS * STEPS)
                        for t in range(NT):
                            for i in range(4):
                                last = pe.matmul(ps[:, t // 4, P * (t % 4):P * (t % 4) + P], G[:, i, t * P:(t + 1) * P],
                                                 w_fo[:, i // 2, i % 2, :], start=(i == 0), stop=(i == 3))
                            last.then_inc(o_ps, 1)
                        pe.wait_ge(y_fin, DIRS * CH * H2)
                        pe.wait_ge(gn_stats, 1)
                        if attn:
                            pe.wait_ge(t2_done, NT)
                        pe.matmul(ps[:, 7, 0:2], gavg[:, :], mv[:, 3, 0, :], start=True, stop=True).then_inc(gn_avg, 1)
                    if attn:
                        turn(lambda t: X3[:, t * P:(t + 1) * P], 3, P, lambda t: pe.wait_ge(x3_ready, t + 1), x3t_ps)
                        pe.wait_ge(x3t_ev, len(TC))
                        pe.wait_ge(exp_done, NP)
                        for t in range(NT):
                            last = pe.matmul(ps[:, 6, EXPERTS * t:EXPERTS * (t + 1)], X3T[:, t * P:(t + 1) * P], rw[:, :],
                                             start=True, stop=True)
                        last.then_inc(lg_ps, 1)
                    if mamba:
                        pe.wait_ge(gn_stats, 2)
                        pe.matmul(ps[:, 7, 0:1], gavg[:, :], gsm[:, 1:2], start=True, stop=True).then_inc(gn_avg, 1)
                        turn(lambda t: YN[:, t * P:(t + 1) * P], 0, P,
                             lambda t: pe.wait_ge(yn_ready, min(4 * (t // 4) + 4, NT)), yt_ps)
                        for t in range(NT):
                            if t % 4 == 0:
                                pe.wait_ge(x1_ready, t // 4 + 1)
                            i = pe.transpose(ps[:, 3 + t // 4, P * (t % 4):P * (t % 4) + P], X[:, t * P:(t + 1) * P],
                                             ident[:, :])
                            if t % 4 == 3 or t == NT - 1:
                                i.then_inc(xt_ps, 1)
                    if attn:
                        pe.wait_ge(pg_ready, 1)
                        if mamba:
                            pe.wait_ge(x1_ready, len(TC))
                        turn(lambda t: PX[:, t, :], 0, 3 * PART, lambda t: None, pt_ps)
                        pe.wait_ge(lg_ready, 1)
                        if mamba:
                            pe.wait_ge(gn_var, 1)
                    if mamba:
                        pe.wait_ge(t1_ev, len(TC))
                        turn(lambda t: XH[:, t, 0:P], 3, P, lambda t: pe.wait_ge(xh_ready, t + 1), xht_ps)

                    def gate_rows(b):
                        i, e = divmod(b, EXPERTS)
                        a, z = TC[i]
                        if b >= 2:
                            pe.wait_ge(xg_done, b - 1)
                        pe.matmul(ps[:, 6 + b % 2, 0:z - a], pick[:, e, :], PTB[:, a:z],
                                  start=True, stop=True).then_inc(e_bc, 1)

                    for part in range(len(TC)):
                        if attn:
                            a, z = TC[part]
                            pe.wait_ge(pt_ev, 2 * len(TC))
                            if part == 0:
                                gate_rows(0)
                            pe.matmul(ps[:, part, 0:z - a], eb[:, :], PT[:, a:z], start=True, stop=False,
                                      skip_group_check=True)
                            pe.wait_ge(t2_copy, 1)
                            for t in range(a // P, z // P):
                                pe.matmul(ps[:, part, t * P - a:t * P - a + P], T2C[:, t * P:(t + 1) * P], ident[:, :],
                                          start=False, stop=False, skip_group_check=True)
                            for e in range(EXPERTS):
                                b = EXPERTS * part + e
                                if b + 1 < EXPERTS * len(TC):
                                    gate_rows(b + 1)
                                pe.wait_ge(xg_done, b + 1)
                                pe.matmul(ps[:, part, 0:z - a], ew[:, e, :], XG[:, b % 2, 0:z - a], start=False,
                                          stop=(e == EXPERTS - 1), skip_group_check=True).then_inc(e_mm, 1)
                        if mamba and part < 2:
                            pe.wait_ge(xht_ev, len(TC))
                            if part == 1:
                                pe.wait_ge(fc_part, len(TC))
                            for i, (a, b) in enumerate(TC):
                                pe.matmul(ps[:, 3 + i, 0:b - a], w1r[:, part, :, :].rearrange("p i a -> p (i a)"),
                                          XHT[:, a:b], start=True, stop=True).then_inc((fr_ps, gr_ps)[part], 1)

                @block.vector
                def _(dve):
                    links = [0]

                    def count(ins):
                        links[0] += 1
                        ins.then_inc(v_link, 1)

                    def link(ins):
                        count(ins)
                        dve.wait_ge(v_link, links[0])

                    def attend(item):
                        if item[0] == "fetch":
                            p = item[1]
                            it, a, b = passes[p]
                            if it >= 1:
                                dve.wait_ge(oo_done, it)
                            dve.wait_ge(et_tr, p + 1)
                            dve.tensor_copy(ET[:, a:b], ps[:, A_BANK, 0:b - a]).then_inc(et_ev, 1)
                        if item[0] == "scale":
                            it = item[1]
                            dve.wait_ge(oo_done, it + 1)
                            link(dve.tensor_scalar(rc[:, 0:1], ps[:, A_BANK, P:P + 1], 1e-10, None, ALU.add))
                            link(dve.reciprocal(rc[:, 1:2], rc[:, 0:1]))
                            dve.scalar_tensor_tensor(T12[:, it * P:(it + 1) * P], ps[:, A_BANK, 0:P], rc[:, 1:2],
                                                     T12[:, it * P:(it + 1) * P], ALU.mult, ALU.add).then_inc(t2_done, 1)

                    def finish_y(q):
                        d, c = divmod(q, CH)
                        dve.wait_ge(y_sum, STATE * (q + 1))
                        for h in range(H2):
                            if q >= 1:
                                dve.wait_ge(g_done, H2 * (q - 1) + h + 1)
                            dve.scalar_tensor_tensor(YT[:, h, 0:SEQ[c] * V], XC[:, h, chunk(c)], dD[:, d, h:h + 1],
                                                     ps[:, Y_BANK + h, 0:SEQ[c] * V], ALU.mult,
                                                     ALU.add).then_inc(y_fin, 1)

                    def copy_b(K):
                        w = SEQ[K % STEPS // STATE] * V
                        dve.wait_ge(b_bc, K + 1)
                        if K >= NBS:
                            dve.wait_ge(dbu_done, K - NBS + 1)
                        dve.tensor_copy(Bs[:, K % NBS, 0:w], ps[:, B_BANK, 0:w]).then_inc(b_ev, 1)

                    def contract(K):
                        c = K % STEPS // STATE
                        w = SEQ[c] * V
                        dve.wait_ge(c_bc, K + 1)
                        dve.wait_ge(scan_done, K + 1)
                        if K >= 2:
                            dve.wait_ge(y_sum, K - 1)
                        dve.tensor_tensor(HC[:, K % 2, 0:2 * w].rearrange("p (h n) -> p h n", h=2),
                                          HS[:, K % 2, 0:2 * w].rearrange("p (h n) -> p h n", h=2),
                                          ps[:, C_BANK + K % 2, 0:w].unsqueeze(1).broadcast_to([P, 2, w]),
                                          ALU.mult).then_inc(hc_done, 1)

                    if mamba:
                        for d in range(DIRS):
                            for u in range(4):
                                dve.wait_ge(th_ready, 4 * d + u + 1)
                                if d == 1 and u == 0:
                                    dve.wait_ge(g_done, H2 * CH)
                                o = (XC if u < 2 else ZS)[:, u % 2, :]
                                dve.scalar_tensor_tensor(o, W[:, 2 + u % 2, :], 1.0, W[:, u % 2, :], ALU.add,
                                                         ALU.mult).then_inc(silu_done, 1)
                            for h in range(H2):
                                for c in range(CH):
                                    j = CH * h + c
                                    dve.wait_ge(dt_ps, H2 * CH * d + j + 1)
                                    dve.tensor_scalar(DT[:, h, chunk(c)], ps[:, (5 * CH + j) % WORK, 0:SEQ[c] * V],
                                                      dtb[:, d, h:h + 1], None, ALU.add).then_inc(x_ready, 1)
                                dve.wait_ge(x_ready, H2 * CH * d + CH * (h + 1))
                                dve.wait_ge(silu_done, 4 * d + 4)
                                dve.tensor_scalar(W[:, 2 + h, :], DT[:, h, :], 80.0, None, ALU.min).then_inc(tm_ready, 1)
                            dve.wait_ge(bc_ev, 2 * CH * (d + 1))
                            link(dve.tensor_tensor(BCF, BCF, S3[:, :], ALU.subtract))
                            dve.tensor_copy(S3[BC:2 * BC, :], BCF[BC:2 * BC, :]).then_inc(s3_ready, 1)
                            link(dve.tensor_copy(S3m[2 * BC:, :], BCF[2 * BC:3 * BC, :]))
                            dve.tensor_tensor(S3[2 * BC:, :], BCF[2 * BC:3 * BC, :], S3m[2 * BC:, :],
                                              ALU.subtract).then_inc(s3_ready, 1)
                            for h in range(H2):
                                dve.wait_ge(sp_ready, H2 * d + h + 1)
                                dve.tensor_tensor(DT[:, h, :], DT[:, h, :], W[:, 2 + h, :], ALU.max).then_inc(dt_done, 1)
                            for k in range(B_AHEAD):
                                copy_b(STEPS * d + k)
                            for k in range(STEPS + 1):
                                K = STEPS * d + k
                                if k < STEPS:
                                    dve.wait_ge(da_ready, 2 * (K + 1))
                                    dve.wait_ge(dbu_done, K + 1)
                                    if K >= 2:
                                        dve.wait_ge(hc_done, K - 1)
                                    w = SEQ[k // STATE] * V
                                    dve.tensor_tensor_scan(HS[:, K % 2, 0:2 * w], DA[:, K % 2, 0:2 * w],
                                                           DBU[:, K % 2, 0:2 * w], 0.0, ALU.mult,
                                                           ALU.add).then_inc(scan_done, 1)
                                if k % STATE == 2 and k > STATE:
                                    finish_y(CH * d + k // STATE - 1)
                                if k >= 1:
                                    contract(K - 1)
                                if k + B_AHEAD < STEPS:
                                    copy_b(K + B_AHEAD)
                                for item in by_step[d * (STEPS + 1) + k]:
                                    attend(item)
                            finish_y(CH * d + CH - 1)
                    chain_end(attend)

                    def stats(i, ready, src, eps, done):
                        for t in range(NT):
                            ready(t)
                            count(dve.bn_stats(st[:, i, t, :], src(t)))
                        first = links[0] - NT
                        for t in range(NT):
                            dve.wait_ge(v_link, first + t + 1)
                            count(dve.bn_aggr(mv[:, i, t, :], st[:, i, t, :]))
                        dve.wait_ge(v_link, links[0])
                        dve.tensor_scalar(va[:, i, :], mv[:, i, :, 1], eps, None, ALU.add).then_inc(done, 1)

                    def normalise(i, ready, src, dst, done):
                        dve.wait_ge(ready, 1)
                        for t in range(NT):
                            dve.tensor_scalar(dst(t), src(t), mv[:, i, t, 0:1], rs[:, i, t:t + 1], ALU.subtract,
                                              ALU.mult).then_inc(done, 1)

                    def tile(a):
                        return lambda t: a[:, t * P:(t + 1) * P]

                    def o_tile(t):
                        return ps[:, t // 4, P * (t % 4):P * (t % 4) + P]

                    if attn:
                        stats(0, lambda t: dve.wait_ge(t2_done, t + 1), tile(T12), 1e-5, var_x)
                    if mamba:
                        stats(1, lambda t: dve.wait_ge(o_ps, min(4 * (t // 4) + 4, NT)), o_tile, 1e-5, var_y)
                    if attn:
                        if mamba:
                            dve.wait_ge(g_done, DIRS * CH * H2)
                        normalise(0, rstd_x, tile(T12), tile(X3), x3_ready)
                    if mamba:
                        normalise(1, rstd_y, o_tile, tile(YN), yn_ready)
                        dve.wait_ge(s_x, 16)
                        q4 = TOK // 4
                        for i in range(4):
                            count(dve.bn_stats(st[:, 3, i, :], XL[:, i * q4:(i + 1) * q4]))
                        dve.wait_ge(v_link, links[0])
                        dve.bn_aggr(mv[:, 3, 0, :], st[:, 3, 0:4, :].rearrange("p a b -> p (a b)")).then_inc(gn_stats, 1)
                        dve.wait_ge(gn_avg, 1)
                        link(dve.tensor_copy(gm[:, :], ps[:, 7, 0:2]))
                        link(dve.tensor_tensor(gsm[:, 0:1], mv[:, 3, 0, 0:1], gm[:, 0:1], ALU.subtract))
                        dve.tensor_tensor(gsm[:, 1:2], gsm[:, 0:1], gsm[:, 0:1], ALU.mult).then_inc(gn_stats, 1)
                    if attn:
                        dve.wait_ge(lg_ps, 1)
                        link(dve.tensor_tensor(LG[...], ps[:, 6, 0:NT * EXPERTS].rearrange("p (t e) -> p t e", e=EXPERTS),
                                               rb[:, :].unsqueeze(1).broadcast_to([P, NT, EXPERTS]), ALU.add))
                        link(dve.tensor_reduce(MX, LG[...], AX.X, ALU.max))
                        dve.tensor_tensor(LP[...], LG[...], MX.unsqueeze(2).broadcast_to([P, NT, EXPERTS]),
                                          ALU.subtract).then_inc(lg_ready, 1)
                    if mamba:
                        dve.wait_ge(gn_avg, 2)
                        dve.scalar_tensor_tensor(gsm[:, 2:3], ps[:, 7, 0:1], 1e-5, gm[:, 1:2], ALU.add,
                                                 ALU.add).then_inc(gn_var, 1)
                        for i, (a, b) in enumerate(TC):
                            dve.wait_ge(yt_ps, i + 1)
                            dve.scalar_tensor_tensor(X[:, a:b], ps[:, i, 0:b - a], lnw[:, 0:1], X[:, a:b], ALU.mult,
                                                     ALU.add).then_inc(x1_ready, 1)
                    if attn:
                        shape = [P, NT, EXPERTS, EXPERTS]
                        other = LG[...].unsqueeze(2).broadcast_to(shape)
                        own = LG[...].unsqueeze(3).broadcast_to(shape)
                        cmp4 = CMP.rearrange("p (t e) f -> p t e f", e=EXPERTS)
                        cmq4 = CMQ.rearrange("p (t e) f -> p t e f", e=EXPERTS)
                        count(dve.tensor_tensor(cmp4, other, own, ALU.is_gt))
                        link(dve.tensor_tensor(cmq4, other, own, ALU.is_equal))
                        link(dve.tensor_tensor(cmq4, cmq4, earlier[...].unsqueeze(1).broadcast_to(shape), ALU.mult))
                        link(dve.tensor_tensor(CMP, CMP, CMQ, ALU.add))
                        link(dve.tensor_reduce(RK, CMP, AX.X, ALU.add))
                        dve.wait_ge(pexp, 1)
                        link(dve.scalar_tensor_tensor(LP[...], RK.rearrange("p (t e) -> p t e", e=EXPERTS), 1.5,
                                                      LP[...], ALU.is_lt, ALU.mult))
                        link(dve.tensor_reduce(MX, LP[...], AX.X, ALU.add))
                        link(dve.reciprocal(MX, MX))
                        link(dve.tensor_tensor(LP[...], LP[...], MX.unsqueeze(2).broadcast_to([P, NT, EXPERTS]),
                                               ALU.mult))
                        link(dve.tensor_copy(LB[...], LP[...]))
                        dve.wait_ge(px_zero, 1)
                        count(dve.tensor_copy(PX[:, :, 0:EXPERTS], LB[...]))
                        link(dve.tensor_tensor(LP[...], LP[...], LB[...], ALU.subtract))
                        link(dve.tensor_copy(LB[...], LP[...]))
                        count(dve.tensor_copy(PX[:, :, PART:PART + EXPERTS], LB[...]))
                        dve.wait_ge(v_link, links[0])
                        dve.tensor_tensor(PX[:, :, 2 * PART:2 * PART + EXPERTS], LP[...], LB[...],
                                          ALU.subtract).then_inc(pg_ready, 1)
                    if mamba:
                        stats(2, lambda t: dve.wait_ge(t1_ev, t // 4 + 1), tile(T12), 1e-5, var_t)
                        dve.wait_ge(gn_rstd, 1)
                        dve.tensor_scalar(XP[:, :, PAD:PAD + V], XL.rearrange("p (s v) -> p s v", v=V), gm[:, 0:1],
                                          gsm[:, 3:4], ALU.subtract, ALU.mult).then_inc(xn_ready, 1)
                        normalise(2, rstd_t, tile(T12), lambda t: XH[:, t, 0:P], xh_ready)

                    for part in range(len(TC)):
                        if attn:
                            a, z = TC[part]
                            for b in range(EXPERTS * part, EXPERTS * (part + 1)):
                                dve.wait_ge(e_bc, b + 1)
                                if b >= 2:
                                    dve.wait_ge(e_mm, b - 1)
                                dve.tensor_tensor(XG[:, b % 2, 0:z - a], X3T[:, a:z], ps[:, 6 + b % 2, 0:z - a],
                                                  ALU.mult).then_inc(xg_done, 1)
                        if mamba and part == 0:
                            for i, (a, b) in enumerate(TC):
                                dve.wait_ge(fr_ps, i + 1)
                                ft = FT[:, a:b].rearrange("p (b i) -> p b i", i=IB)
                                dve.tensor_tensor(ft, ps[:, 3 + i, 0:b - a].rearrange("p (b i) -> p b i", i=IB),
                                                  mask8[:, :].unsqueeze(1).broadcast_to([P, (b - a) // IB, IB]),
                                                  ALU.mult).then_inc(fc_part, 1)
                                dve.wait_ge(fc_part, i + 1)
                                link(dve.tensor_reduce(FC[:, a // IB:b // IB], ft, AX.X, ALU.add))
                            dve.tensor_scalar(FC[:, :], FC[:, :], b1c[:, 0:1], None, ALU.add).then_inc(fc_ready, 1)

            nc.all_engine_barrier(sems_to_clear=range(nums[0], nums[-1] + 1))

        with nc.Block() as block:
            @block.sync
            def _(sp):
                sp.dma_start(XL, x[0:1].rearrange("a p t v -> p (a t v)")).then_inc(s_x, 16)

            @block.tensor
            def _(pe):
                pe.wait_ge(gn_stats, 1)
                pe.matmul(ps[:, 7, 0:2], gavg[:, :], mv[:, 3, 0, :], start=True, stop=True).then_inc(gn_avg, 1)
                pe.wait_ge(gn_stats, 2)
                pe.matmul(ps[:, 7, 0:1], gavg[:, :], gsm[:, 1:2], start=True, stop=True).then_inc(gn_avg, 1)

            @block.gpsimd
            def _(pool):
                pool.wait_ge(gn_var, 1)
                pool.tensor_tensor(gsm[:, 3:4], gsm[:, 2:3], mhalf[:, 0:1], ALU.pow).then_inc(gn_rstd, 1)
                pool.tensor_scalar(X[:, :], XL, lnb[:, 0:1], None, ALU.add).then_inc(xb_ready, 1)

            @block.vector
            def _(dve):
                dve.wait_ge(s_x, 16)
                q4 = TOK // 4
                for i in range(4):
                    dve.bn_stats(st[:, 3, i, :], XL[:, i * q4:(i + 1) * q4]).then_inc(v_link, 1)
                dve.wait_ge(v_link, 4)
                dve.bn_aggr(mv[:, 3, 0, :], st[:, 3, 0:4, :].rearrange("p a b -> p (a b)")).then_inc(gn_stats, 1)
                dve.wait_ge(gn_avg, 1)
                dve.tensor_copy(gm[:, :], ps[:, 7, 0:2]).then_inc(v_link, 1)
                dve.wait_ge(v_link, 5)
                dve.tensor_tensor(gsm[:, 0:1], mv[:, 3, 0, 0:1], gm[:, 0:1], ALU.subtract).then_inc(v_link, 1)
                dve.wait_ge(v_link, 6)
                dve.tensor_tensor(gsm[:, 1:2], gsm[:, 0:1], gsm[:, 0:1], ALU.mult).then_inc(gn_stats, 1)
                dve.wait_ge(gn_avg, 2)
                dve.scalar_tensor_tensor(gsm[:, 2:3], ps[:, 7, 0:1], 1e-5, gm[:, 1:2], ALU.add, ALU.add).then_inc(gn_var, 1)
                dve.wait_ge(gn_rstd, 1)
                dve.tensor_scalar(XP[:, :, PAD:PAD + V], XL.rearrange("p (s v) -> p s v", v=V), gm[:, 0:1],
                                  gsm[:, 3:4], ALU.subtract, ALU.mult).then_inc(xn_ready, 1)
        nc.all_engine_barrier(sems_to_clear=range(nums[0], nums[-1] + 1))

        body(0, True, False)
        if NM > 1:
            with nc.Fori(1, NM) as n:
                body(n, True, True)
        body(NM, False, True)


def kernel(**inputs):
    import numpy as np
    import concourse.bacc as bacc
    from concourse import mybir as _mybir
    from concourse.bass_utils import run_bass_kernel_spmd

    def get(name):
        return np.asarray(inputs[name])

    def both(name, turn=False):
        pair = [get(f"L0_conv_{p}_{name}") for p in "fb"]
        return np.stack([w.T if turn else w for w in pair])

    arrays = {
        "x": get("x"),
        "in_wT": both("in_w", True),
        "conv_wT": both("conv_w", True).reshape(2, -1),
        "conv_b": both("conv_b"),
        "xproj_w": both("xproj_w"),
        "xprojT": both("xproj_w", True),
        "dt_wT": both("dt_w", True),
        "dt_b": both("dt_b"),
        "Alog": both("Alog"),
        "Dp": both("D"),
        "out_w": both("out_w"),
        "fuseT": get("L0_conv_fuse_w").T,
        "ln_w": get("L0_conv_ln_w"),
        "ln_b": get("L0_conv_ln_b"),
        "W1": get("L1_attn_W1"),
        "b1t": np.tile(get("L1_attn_b1"), 8),
        "w2t": np.tile(get("L1_attn_w2")[:, 0], 8),
        "b2": get("L1_attn_b2"),
        "router_w": get("L1_ffn_router_w"),
        "router_b": get("L1_ffn_router_b"),
        "expert_w": get("L1_ffn_expert_w"),
        "expert_b": get("L1_ffn_expert_b"),
    }
    nc = bacc.Bacc("TRN2", target_bir_lowering=False, num_devices=1)
    feeds, args = {}, []
    for name, a in arrays.items():
        a = np.ascontiguousarray(a)
        feeds[f"in_{name}"] = a
        args.append(nc.dram_tensor(f"in_{name}", a.shape, _mybir.dt.from_np(a.dtype), kind="ExternalInput").ap())
    out = nc.dram_tensor("out", arrays["x"].shape, F32, kind="ExternalOutput").ap()
    hybrid_kernel(nc, *args, out)
    r = run_bass_kernel_spmd(nc, [feeds], core_ids=[0])
    return r.results[0]["out"]
```
